# Optimizing a Trainium2 kernel written in Bass

```python
import numpy as np
import jax
import jax.numpy as jnp

def _softmax(x, axis=-1):
    return jax.nn.softmax(x, axis=axis)

def _gelu(x):
    return jax.nn.gelu(x, approximate=True)

def _silu(x):
    return jax.nn.silu(x)

def _sigmoid(x):
    return jax.nn.sigmoid(x)

def _layernorm(x, axis=-1, eps=1e-05):
    m = jnp.mean(x, axis=axis, keepdims=True)
    v = jnp.var(x, axis=axis, keepdims=True)
    return (x - m) / jnp.sqrt(v + eps)

def _scatter_add(tgt, idx, src, axis=0):
    return tgt.at[idx].add(src)

def _segment_sum(src, seg, n):
    return jax.ops.segment_sum(src, seg, n)
kernel_name = 'mk_seq_preln_d1_jaxref_r4_e393f2'

def setup_inputs(seed: int=0):
    np.random.seed(seed)
    _w = jnp.asarray

    def _L0_attn_setup():
        import math
        import jax, jax.numpy as jnp
        import numpy as np
        N_HEAD = 16

        def _reference_tuple_inner(x, W_dq, W_uq, W_dkv, W_uk, W_uv, W_o):
            B, T, C = x.shape
            nh = N_HEAD
            hs = C // nh
            kvl = W_dkv.shape[0]
            k_eff = (W_dq.T @ W_uq.T @ W_uk).reshape(nh, hs, kvl)
            v_eff = (W_uv.T @ W_o.T).reshape(kvl, nh, hs).transpose(1, 0, 2)
            c_kv = x @ W_dkv.T
            q = (x @ W_dq.T @ W_uq.T).reshape(B, T, nh, hs).transpose(0, 2, 1, 3)
            q_lat = jnp.einsum('bhtd,hdl->bhtl', q, k_eff)
            attn = jnp.einsum('bhtl,bsl->bhts', q_lat, c_kv) / math.sqrt(hs)
            causal_mask = jnp.triu(jnp.ones((T, T), bool), k=1)
            attn = jnp.where(causal_mask[None, None], -jnp.inf, attn)
            attn = jax.nn.softmax(attn, axis=-1)
            ctx = jnp.einsum('bhts,bsl->bhtl', attn, c_kv)
            y = jnp.einsum('bhtl,hld->bhtd', ctx, v_eff).transpose(0, 2, 1, 3).reshape(B, T, C)
            return (y, c_kv)
        key = jax.random.key(seed)
        ks = jax.random.split(key, 7)
        B, T, C = (4, 512, 256)
        QL, KVL = (64, 64)
        s = 0.02
        return {'x': jax.random.normal(ks[0], (B, T, C), jnp.float32), 'W_dq': jax.random.normal(ks[1], (QL, C), jnp.float32) * s, 'W_uq': jax.random.normal(ks[2], (C, QL), jnp.float32) * s, 'W_dkv': jax.random.normal(ks[3], (KVL, C), jnp.float32) * s, 'W_uk': jax.random.normal(ks[4], (C, KVL), jnp.float32) * s, 'W_uv': jax.random.normal(ks[5], (C, KVL), jnp.float32) * s, 'W_o': jax.random.normal(ks[6], (C, C), jnp.float32) * s}
    _L0_attn_in = _L0_attn_setup()

    def _L0_ffn_setup():
        import jax, jax.numpy as jnp
        import numpy as np
        D_MODEL = 256
        key = jax.random.key(seed)
        k_x, k_w, k_a1, k_a2 = jax.random.split(key, 4)
        x = jax.random.normal(k_x, (4, 512, D_MODEL), dtype=jnp.float32)
        weight = jax.random.normal(k_w, (D_MODEL, D_MODEL), dtype=jnp.float32) * 0.02
        aux_weight1 = jax.random.normal(k_a1, (D_MODEL, D_MODEL), dtype=jnp.float32) * 0.02
        aux_weight2 = jax.random.normal(k_a2, (D_MODEL, D_MODEL), dtype=jnp.float32) * 0.02
        bias = jnp.zeros((D_MODEL,), dtype=jnp.float32)
        return {'x': x, 'weight': weight, 'aux_weight1': aux_weight1, 'aux_weight2': aux_weight2, 'bias': bias}
    _L0_ffn_in = _L0_ffn_setup()
    _d = {'L0_attn_x': _L0_attn_in['x'], 'L0_attn_W_dq': _L0_attn_in['W_dq'], 'L0_attn_W_uq': _L0_attn_in['W_uq'], 'L0_attn_W_dkv': _L0_attn_in['W_dkv'], 'L0_attn_W_uk': _L0_attn_in['W_uk'], 'L0_attn_W_uv': _L0_attn_in['W_uv'], 'L0_attn_W_o': _L0_attn_in['W_o'], 'L0_ffn_weight': _L0_ffn_in['weight'], 'L0_ffn_aux_weight1': _L0_ffn_in['aux_weight1'], 'L0_ffn_aux_weight2': _L0_ffn_in['aux_weight2'], 'L0_ffn_bias': _L0_ffn_in['bias']}
    _x0 = _d['L0_attn_x']
    _d['L0_attn_x'] = jax.random.normal(jax.random.fold_in(jax.random.key(seed), 1), (32, 512, 256), dtype=_x0.dtype)
    del _x0
    return _d

def reference(L0_attn_x, L0_attn_W_dq, L0_attn_W_uq, L0_attn_W_dkv, L0_attn_W_uk, L0_attn_W_uv, L0_attn_W_o, L0_ffn_weight, L0_ffn_aux_weight1, L0_ffn_aux_weight2, L0_ffn_bias):

    def _L0_attn_ref(x, W_dq, W_uq, W_dkv, W_uk, W_uv, W_o):
        import math
        import jax, jax.numpy as jnp
        import numpy as np
        N_HEAD = 16

        def _reference_tuple_inner(x, W_dq, W_uq, W_dkv, W_uk, W_uv, W_o):
            B, T, C = x.shape
            nh = N_HEAD
            hs = C // nh
            kvl = W_dkv.shape[0]
            k_eff = (W_dq.T @ W_uq.T @ W_uk).reshape(nh, hs, kvl)
            v_eff = (W_uv.T @ W_o.T).reshape(kvl, nh, hs).transpose(1, 0, 2)
            c_kv = x @ W_dkv.T
            q = (x @ W_dq.T @ W_uq.T).reshape(B, T, nh, hs).transpose(0, 2, 1, 3)
            q_lat = jnp.einsum('bhtd,hdl->bhtl', q, k_eff)
            attn = jnp.einsum('bhtl,bsl->bhts', q_lat, c_kv) / math.sqrt(hs)
            causal_mask = jnp.triu(jnp.ones((T, T), bool), k=1)
            attn = jnp.where(causal_mask[None, None], -jnp.inf, attn)
            attn = jax.nn.softmax(attn, axis=-1)
            ctx = jnp.einsum('bhts,bsl->bhtl', attn, c_kv)
            y = jnp.einsum('bhtl,hld->bhtd', ctx, v_eff).transpose(0, 2, 1, 3).reshape(B, T, C)
            return (y, c_kv)
        return _reference_tuple_inner(x, W_dq, W_uq, W_dkv, W_uk, W_uv, W_o)[0]

    def _L0_ffn_ref(x, weight, aux_weight1, aux_weight2, bias):
        import jax, jax.numpy as jnp
        import numpy as np
        D_MODEL = 256
        h = jnp.einsum('btc,cd->btd', x, weight)
        h = jnp.einsum('btc,cd->btd', h, aux_weight1)
        h = jnp.einsum('btc,cd->btd', h, aux_weight2)
        return jnp.tanh(h + bias)
    x = L0_attn_x
    x = x + _L0_attn_ref(_layernorm(x, axis=-1), L0_attn_W_dq, L0_attn_W_uq, L0_attn_W_dkv, L0_attn_W_uk, L0_attn_W_uv, L0_attn_W_o)
    x = x + _L0_ffn_ref(_layernorm(x, axis=-1), L0_ffn_weight, L0_ffn_aux_weight1, L0_ffn_aux_weight2, L0_ffn_bias)
    return x

_drawn_inputs = setup_inputs


def setup_inputs(seed=0):
    import zlib

    import numpy as np

    out = dict(_drawn_inputs(seed))
    spreads = {'L0_ffn_bias': (0.0, 2.0)}
    factors = {'L0_attn_W_dq': 8.0,
     'L0_attn_W_uq': 8.0,
     'L0_attn_W_dkv': 8.0,
     'L0_attn_W_uk': 8.0,
     'L0_attn_W_uv': 8.0,
     'L0_attn_W_o': 8.0,
     'L0_ffn_weight': 8.0,
     'L0_ffn_aux_weight1': 8.0,
     'L0_ffn_aux_weight2': 8.0}
    for name, (base, spread) in spreads.items():
        noise = np.random.default_rng([zlib.crc32(name.encode()), seed]).standard_normal(out[name].shape)
        drawn = base * np.exp(spread * noise) if base else spread * noise
        out[name] = jnp.asarray(drawn.astype(out[name].dtype))
    for name, factor in factors.items():
        out[name] = (out[name] * factor).astype(out[name].dtype)
    return out
```

```python
from contextlib import ExitStack

import concourse.bass as bass
from concourse import mybir

F32 = mybir.dt.float32
BF16 = mybir.dt.bfloat16
ALU = mybir.AluOpType
ACT = mybir.ActivationFunctionType

P = 128
NH, HS = 16, 16
HQ = 4
NQ = NH // HQ
PARTS = 6
ROWS = PARTS * HS
Q_PART = (0, 0, 1, 1, 0, 2)
K_PART = (0, 1, 0, 1, 2, 0)
PAIRS = 5
UNITS = 10
EPS = 1e-5
MASKED = -3.0e38

FILLS = (
    (0, 0, "A xT0"), (0, 1, "A xT1"), (0, 2, "M 0"), (0, 3, "A down"), (0, 4, "A qk0"),
    (1, 0, "A qk1"), (1, 1, "A qk2"), (1, 2, "A qk3"), (1, 2, "M 1"), (1, 3, "D y0"), (1, 4, "D y1"),
    (2, 0, "D y2"), (2, 1, "D y3"), (2, 2, "M 2"), (2, 3, "A v0"), (2, 4, "A v1"),
    (3, 1, "D xT0"), (3, 2, "D xT1"), (3, 2, "M 3"), (3, 3, "D f0"), (3, 4, "D f1"),
)
Y_SLOTS = [f[:2] for f in FILLS if f[2][:3] == "D y"]
A_FILLS = [f[2] for f in FILLS if f[2][0] == "A"]
D_FILLS = [f[2] for f in FILLS if f[2][0] == "D"]


def block_kernel(nc, x, w_down, w_uq, w_uqT, w_uk, w_dq, w_uv, w_oT, w_1T, w_a1, w_a2, bias, out):
    NB, T, C = x.shape
    NT = T // P
    CT = C // P
    L = w_uk.shape[1]
    SCALE = float(HS) ** -0.5
    assert (NT, CT, L) == (4, 2, 64)

    def known(k):
        return isinstance(k, int)

    def fills(k):
        return [f[2] for f in FILLS if not (f[2][0] == "A" and known(k) and k == NB - 1)
                and not (f[2][0] == "D" and known(k) and k == 0)]

    def fill_no(k, name):
        if known(k) and k == -1:
            return A_FILLS.index(name)
        base = len(A_FILLS)
        if known(k) and k == 0:
            return base + fills(0).index(name)
        base += len(fills(0))
        if known(k) and k == NB:
            return base + len(FILLS) * (NB - 2) + len(fills(NB - 1)) + D_FILLS.index(name)
        return (k - 1) * len(FILLS) + base + fills(k).index(name)

    def wait(eng, sem, value):
        if not known(value) or value > 0:
            eng.wait_ge(sem, value)

    def wait_apart(eng, sem, value, passed):
        eng.wait_ge(sem, value)
        if not known(value):
            eng.sem_inc(passed, 1)

    with ExitStack() as ctx:
        def sb(name, shape, dt=F32):
            return ctx.enter_context(nc.sbuf_tensor(name, shape, dt))

        def pb(name, shape, dt=F32):
            return ctx.enter_context(nc.psum_tensor(name, shape, dt))

        def sem(name):
            return ctx.enter_context(nc.semaphore(name))

        wd = sb("wd", [P, CT, P])
        wuq = sb("wuq", [P, CT, L])
        wuk = sb("wuk", [P, CT, L])
        wdq = sb("wdq", [L, C])
        wuv = sb("wuv", [P, CT, L])
        woT = sb("woT", [P, CT, C])
        w1T = sb("w1T", [P, CT, C])
        wa1 = sb("wa1", [P, CT, C])
        wa2 = sb("wa2", [P, CT, C])
        gqk = sb("gqk", [L, L])
        m1T = sb("m1T", [P, CT, C])
        wf = sb("wf", [P, CT, C])
        wq = sb("wq", [P, C])
        wk = sb("wk", [P, C])
        wv = sb("wv", [P, C])
        bias_b = sb("bias_b", [P, 2, C])
        ident = sb("ident", [P, P])
        ident_b = sb("ident_b", [P, P], BF16)
        causal = sb("causal", [P, T])
        after = sb("after", [P, 2, P], BF16)
        half = sb("half", [P, NT])
        xin = sb("xin", [P, NT, C])
        xres = sb("xres", [P, NT, C])
        stats = sb("stats", [P, NT, 6])
        mv = sb("mv", [P, NT, 2])
        ve = sb("ve", [P, NT])
        rstd = sb("rstd", [P, NT])
        shift = sb("shift", [P, NT])
        nshift = sb("nshift", [P, NT])
        xn = sb("xn", [P, NT, C])
        xnT = sb("xnT", [P, CT, T])
        downT = sb("downT", [P, T])
        part = [[sb(f"{n}part{i}", [P, 2, T], BF16) for i in range(3)] for n in "qk"]
        rest = [[sb(f"{n}rest{g}", [P, T]) for g in range(2)] for n in "qk"]
        qs = [sb(f"qs{i}", [P, NH, T], BF16) for i in range(2)]
        ks = [sb(f"ks{i}", [P, NH, T], BF16) for i in range(2)]
        vv = [sb(f"vv{i}", [P, NT, NH, 32]) for i in range(2)]
        mx = sb("mx", [P, NQ, NT, HQ])
        scrap = sb("scrap", [P, 2, T])
        nm = sb("nm", [P, 2, NT, 3, HQ], BF16)
        nr = sb("nr", [P, 2, 2, NT, HQ])
        nmT = sb("nmT", [3 * HQ, 2, T], BF16)
        probs = [sb(f"probs{u}", [P, 2, T]) for u in range(PAIRS)]
        yT = sb("yT", [P, NQ, T])
        rden = sb("rden", [P, 2, NH])
        yb = sb("yb", [P, NT, C])
        x1 = sb("x1", [P, NT, C])
        stats2 = sb("stats2", [P, NT, 6])
        mv2 = sb("mv2", [P, NT, 2])
        ve2 = sb("ve2", [P, NT])
        rstd2 = sb("rstd2", [P, NT])
        shift2 = sb("shift2", [P, NT])
        nshift2 = sb("nshift2", [P, NT])
        xn2 = sb("xn2", [P, NT, C])
        xn2T = sb("xn2T", [P, CT, T])
        hb = sb("hb", [P, 2, 2, C])
        th = sb("th", [P, 2, 2, C])
        xo = sb("xo", [P, 2, 2, C])

        st_ps = pb("st_ps", [P, 2, 2, T])
        s_ps = pb("s_ps", [P, 2, T])
        pv_ps = pb("pv_ps", [P, T])
        sh_ps = pb("sh_ps", [P, T])
        sh_bf = sh_ps[:].bitcast(BF16)

        w_in = sem("w_in")
        dve_passed = sem("dve_passed")
        pool_passed = sem("pool_passed")
        consts = sem("consts")
        tri0 = sem("tri0")
        prep_mm = sem("prep_mm")
        prep_out = sem("prep_out")
        x_in = sem("x_in")
        r_in = sem("r_in")
        stat1, mv1 = sem("stat1"), sem("mv1")
        pool1 = sem("pool1")
        xn_ok = sem("xn_ok")
        filled = sem("filled")
        emptied = sem("emptied")
        hi_ok = sem("hi_ok")
        mid_ok = sem("mid_ok")
        low_ok = sem("low_ok")
        stacked = sem("stacked")
        s_full = sem("s_full")
        s_read = sem("s_read")
        neg = sem("neg")
        max_in = [sem(f"max_in{i}") for i in range(2)]
        st_full = sem("st_full")
        exp_ok = sem("exp_ok")
        pv_ok = sem("pv_ok")
        yT_ok = sem("yT_ok")
        rden_ok = sem("rden_ok")
        x1_ok = sem("x1_ok")
        stat2, mv2_ok = sem("stat2"), sem("mv2_ok")
        pool2 = sem("pool2")
        xn2_ok = sem("xn2_ok")
        th_ok = sem("th_ok")
        xo_ok = sem("xo_ok")
        xo_out = [sem(f"xo_out{i}") for i in range(2)]
        N_W = 12

        block = ctx.enter_context(nc.Block())

        def programme(eng, prelude, step, tail):
            prelude()
            step(-1, 3, 1)
            for s in range(4):
                step(0, s, 0)
            with eng.Fori(0, (NB - 4) // 2) as i:
                for odd in range(2):
                    for s in range(4):
                        step(i * 2 + 1 + odd, s, 1 - odd)
            for k in range(NB - 3, NB):
                for s in range(4):
                    step(k, s, k % 2)
            step(NB, 0, 0)
            tail()

        def has(k, s):
            if not known(k):
                return True, True, True
            n = 4 * k + s
            return 0 <= n - 1 < NQ * NB, 0 <= n < NQ * NB, 0 <= n + 1 < NQ * NB

        def has_pv(k, s):
            return not known(k) or 0 <= 4 * k + s - 2 < NQ * NB

        def has_batch(b):
            return not known(b) or 0 <= b < NB

        def jobs(k):
            if not known(k):
                return True, True
            return 0 <= k < NB - 1, 1 <= k < NB

        def step_fills(k, s, u):
            if known(k) and k in (-1, NB):
                return []
            return [f[2] for f in FILLS if f[:2] == (s, u) and f[2] in fills(k)]

        @block.sync
        def _(sp):
            def load_x(b):
                wait(sp, xn_ok, b)
                sp.dma_start(xin[:], x[b].rearrange("(t p) c -> p t c", p=P)).then_inc(x_in, 16)

            def load_res(b):
                sp.dma_start(xres[:], x[b].rearrange("(t p) c -> p t c", p=P)).then_inc(r_in, 16)

            def stack_parts(b, par, which):
                stack, order = ((qs, Q_PART), (ks, K_PART))[which]
                if which == 0:
                    wait(sp, st_full, (b - 1) * (PAIRS * NQ))
                for r, p in sorted(enumerate(order), key=lambda a: a[1]):
                    sp.wait_ge((hi_ok, mid_ok, low_ok)[p], b * 4 + 2 * (which + 1))
                    sp.dma_start(stack[par][HS * r:HS * (r + 1), :, :], part[which][p][:])\
                        .then_inc(stacked, 16)

            def max_rows(k, s, par):
                sp.wait_ge(emptied, fill_no(k, f"M {s}") + 1)
                sp.dma_start(qs[par][ROWS:ROWS + 3, HQ * s:HQ * (s + 1), :], nmT[:, s % 2, :])\
                    .then_inc(max_in[s % 2], 16)

            def store(b, f):
                sp.wait_ge(xo_ok, b * 2 + (f + 1))
                sp.dma_start(out[b, 2 * f * P:2 * (f + 1) * P, :].rearrange("(t p) c -> p t c", p=P),
                             xo[:, f]).then_inc(xo_out[f], 16)

            def prelude():
                load_x(0)
                for dst, src in ((wd, w_down), (wuq, w_uq), (wuk, w_uk), (wuv, w_uv), (woT, w_oT),
                                 (w1T, w_1T), (wa1, w_a1), (wa2, w_a2)):
                    sp.dma_start(dst[:], src.rearrange("(t p) n -> p t n", p=P)).then_inc(w_in, 16)
                sp.dma_start(wdq[:], w_dq).then_inc(w_in, 16)
                for t in range(2):
                    sp.dma_start(bias_b[:, t, :], bias.partition_broadcast(P)).then_inc(w_in, 16)
                sp.wait_ge(consts, 1)
                sp.dma_start(wq[0:L, :], w_uqT).then_inc(w_in, 16)
                load_x(1)
                stack_parts(0, 0, 0)
                stack_parts(0, 0, 1)

            def step(k, s, par):
                _, mt, _ = has(k, s)
                a, d = jobs(k)
                if s == 0 and mt:
                    if has_batch(k + 2):
                        load_x(k + 2)
                    if d:
                        load_res(k - 1)
                if s == 1 and a:
                    stack_parts(k + 1, 1 - par, 0)
                if mt:
                    max_rows(k, s, par)
                if s == 1 and a:
                    stack_parts(k + 1, 1 - par, 1)
                if s == 3 and d:
                    store(k - 1, 0)
                    store(k - 1, 1)

            def tail():
                load_res(NB - 1)
                store(NB - 1, 0)
                store(NB - 1, 1)
                for f in range(2):
                    sp.wait_ge(xo_out[f], 16 + 16 * NB)

            programme(sp, prelude, step, tail)

        @block.gpsimd
        def _(pool):
            passed = pool_passed

            def prelude():
                for t in (wk, wv, wq, ident, ident_b, causal, after):
                    nc.gpsimd.memset(t[:], 0.0)
                for i in range(2):
                    for t in (qs[i], ks[i], vv[i]):
                        nc.gpsimd.memset(t[:], 0.0)
                nc.gpsimd.memset(half[:], -0.5).then_inc(tri0, 1)
                pool.wait_ge(tri0, 1)
                for i in range(2):
                    nc.gpsimd.memset(ks[i][ROWS:ROWS + 3, :, :], 1.0).then_inc(tri0, 1)
                    pool.wait_ge(tri0, i + 2)
                for i in range(2):
                    nc.gpsimd.memset(vv[i][:, :, :, HS:HS + 1], 1.0)
                for t in (ident, ident_b):
                    nc.gpsimd.affine_select(out=t[:], in_=t[:], compare_op=ALU.not_equal, fill=1.0, base=0,
                                            pattern=[[-1, P]], channel_multiplier=1)
                nc.gpsimd.affine_select(out=after[:], in_=after[:], compare_op=ALU.is_ge, fill=MASKED, base=0,
                                        pattern=[[0, 2], [1, P]], channel_multiplier=-1)
                tri = causal[:, T - P:T]
                nc.gpsimd.affine_select(out=tri, in_=tri, compare_op=ALU.is_ge, fill=MASKED, base=0,
                                        pattern=[[-1, P]], channel_multiplier=1).then_inc(consts, 1)
                for f in range(2):
                    pool.sem_inc(xo_out[f], 16)
                norm1(0)
                for j in range(4):
                    low(0, j)

            def norm(b, src, into, mean_var, done, chain, ok, tmp):
                ve_, rstd_, shift_, nshift_ = tmp
                wait_apart(pool, done, b + 1, passed)
                nc.gpsimd.tensor_scalar(ve_[:], mean_var[:, :, 1], 1.0, EPS, ALU.mult, ALU.add)\
                    .then_inc(chain, 1)
                pool.wait_ge(chain, b * 4 + 1)
                nc.gpsimd.tensor_tensor(rstd_[:], ve_[:], half[:], ALU.pow).then_inc(chain, 1)
                pool.wait_ge(chain, b * 4 + 2)
                nc.gpsimd.tensor_tensor(shift_[:], mean_var[:, :, 0], rstd_[:], ALU.mult).then_inc(chain, 1)
                wait_apart(pool, chain, b * 4 + 3, passed)
                nc.gpsimd.tensor_scalar(nshift_[:], shift_[:], -1.0, 1.0, ALU.mult, ALU.mult)\
                    .then_inc(chain, 1)
                wait_apart(pool, chain, b * 4 + 4, passed)
                for t in range(NT):
                    last = nc.gpsimd.tensor_scalar(into[:, t, :], src[:, t, :], rstd_[:, t:t + 1],
                                                   nshift_[:, t:t + 1], ALU.mult, ALU.add)
                last.then_inc(ok, 1)

            def norm1(b):
                norm(b, xin, xn, mv, mv1, pool1, xn_ok, (ve, rstd, shift, nshift))

            def norm2(b):
                norm(b, x1, xn2, mv2, mv2_ok, pool2, xn2_ok, (ve2, rstd2, shift2, nshift2))

            def low(b, j):
                which, g = j // 2, j % 2
                pool.wait_ge(mid_ok, b * 4 + (j + 1))
                nc.gpsimd.tensor_tensor(part[which][2][:, g, :], rest[which][g][:], part[which][1][:, g, :],
                                        ALU.subtract).then_inc(low_ok, 1)

            def negate(n, s):
                i = s % 2
                m = mx[:, s, :, :]
                wait_apart(pool, s_read, n * UNITS + UNITS, passed)
                nc.gpsimd.tensor_scalar(nm[:, i, :, 0, :], m, -1.0, 1.0, ALU.mult, ALU.mult).then_inc(neg, 1)
                pool.wait_ge(neg, n * 5 + 1)
                nc.gpsimd.tensor_tensor(nr[:, i, 0], m, nm[:, i, :, 0, :], ALU.add).then_inc(neg, 1)
                wait_apart(pool, neg, n * 5 + 2, passed)
                nc.gpsimd.tensor_scalar(nm[:, i, :, 1, :], nr[:, i, 0], -1.0, 1.0, ALU.mult, ALU.mult)\
                    .then_inc(neg, 1)
                pool.wait_ge(neg, n * 5 + 3)
                nc.gpsimd.tensor_tensor(nr[:, i, 1], nr[:, i, 0], nm[:, i, :, 1, :], ALU.add).then_inc(neg, 1)
                wait_apart(pool, neg, n * 5 + 4, passed)
                nc.gpsimd.tensor_scalar(nm[:, i, :, 2, :], nr[:, i, 1], -1.0, 1.0, ALU.mult, ALU.mult)\
                    .then_inc(neg, 1)

            def add_residual(k, t):
                b = k - 1
                pool.wait_ge(emptied, fill_no(k, f"D y{t}") + 1)
                if t == 0:
                    pool.wait_ge(r_in, b * 16 + 16)
                nc.gpsimd.tensor_tensor(x1[:, t, :], yb[:, t, :], xres[:, t, :], ALU.add)\
                    .then_inc(x1_ok, 1)

            def add_ffn(b, f):
                pool.wait_ge(th_ok, b * 2 + (f + 1))
                pool.wait_ge(xo_out[f], b * 16 + 16)
                nc.gpsimd.tensor_tensor(xo[:, f], x1[:, 2 * f:2 * f + 2, :], th[:, f], ALU.add)\
                    .then_inc(xo_ok, 1)

            def step(k, s, par):
                st, mt, _ = has(k, s)
                a, d = jobs(k)
                n = k * 4 + s
                for u in range(PAIRS):
                    if u == 0 and mt:
                        negate(n, s)
                    if a and s == 1 and u < 4:
                        low(k + 1, u)
                    if d and (s, u) in Y_SLOTS:
                        add_residual(k, Y_SLOTS.index((s, u)))
                    if d and (s, u) == (2, 4):
                        norm2(k - 1)
                    if (s, u) == (3, 3) and has_batch(k + 2):
                        norm1(k + 2)
                    if d and (s, u) == (3, 4):
                        add_ffn(k - 1, 0)
                        add_ffn(k - 1, 1)

            def tail():
                for t in range(NT):
                    add_residual(NB, t)
                norm2(NB - 1)
                add_ffn(NB - 1, 0)
                add_ffn(NB - 1, 1)

            programme(pool, prelude, step, tail)

        @block.scalar
        def _(act):
            def copy_out(k, name, dst, src):
                act.wait_ge(filled, fill_no(k, name) + 1)
                nc.scalar.activation(dst, src, ACT.Copy).then_inc(emptied, 1)

            def hi(k, j):
                which, g = j // 2, j % 2
                act.wait_ge(filled, fill_no(k, f"A qk{j}") + 1)
                if j == 0:
                    wait(act, stacked, (k + 1) * (16 * 2 * PARTS))
                nc.scalar.activation(part[which][0][:, g, :], sh_ps[:], ACT.Copy).then_inc(hi_ok, 1)

            def mid(k, j):
                which, g = j // 2, j % 2
                act.wait_ge(emptied, fill_no(k, f"A qk{j}") + 1)
                nc.scalar.activation(part[which][1][:, g, :], rest[which][g][:], ACT.Copy).then_inc(mid_ok, 1)

            def values(k, f, par):
                copy_out(k, f"A v{f}", vv[par][:, 2 * f:2 * f + 2, :, 0:HS],
                         sh_ps[:].rearrange("p (t h d) -> p t h d", t=2, h=NH))

            def prelude():
                copy_out(-1, "A xT0", xnT[:, 0, :], sh_ps[:])
                copy_out(-1, "A xT1", xnT[:, 1, :], sh_ps[:])
                copy_out(-1, "A down", downT[:], sh_ps[:])
                for j in range(4):
                    hi(-1, j)
                    mid(-1, j)
                act.wait_ge(consts, 1)
                values(-1, 0, 0)
                values(-1, 1, 0)

            def exp(n, s, u):
                pair = (n - 1) * PAIRS + u
                act.wait_ge(st_full, pair + 1)
                wait(act, pv_ok, (n - 2) * 3 + (1, 1, 2, 2, 3)[u])
                nc.scalar.activation(probs[u][:], st_ps[:, (s + 1 + u) % 2, :, :], ACT.Exp, scale=SCALE)\
                    .then_inc(exp_ok, 1)

            def outputs(k, s, n):
                act.wait_ge(pv_ok, (n - 2) * 3 + 3)
                if s == 2 and jobs(k)[1]:
                    act.wait_ge(filled, fill_no(k, "D y3") + 1)
                nc.scalar.activation(yT[:, (s - 2) % NQ, :], pv_ps[:], ACT.Copy).then_inc(yT_ok, 1)

            def tanh(k, f):
                act.wait_ge(emptied, fill_no(k, f"D f{f}") + 1)
                nc.scalar.activation(th[:, f], hb[:, f], ACT.Tanh).then_inc(th_ok, 1)

            def step(k, s, par):
                st, mt, _ = has(k, s)
                a, d = jobs(k)
                n = k * 4 + s
                for u in range(PAIRS):
                    if st:
                        exp(n, s, u)
                    if u == 2 and has_pv(k, s):
                        outputs(k, s, n)
                    if u == 2 and a and s == 1:
                        mid(k, 2)
                        hi(k, 3)
                    if u == 2 and d and s == 3:
                        copy_out(k, "D xT1", xn2T[:, 1, :], sh_ps[:])
                    if u == 2 and mt:
                        act.wait_ge(filled, fill_no(k, f"M {s}") + 1)
                        nc.scalar.activation(nmT[:, s % 2, :], sh_bf[0:3 * HQ, 0:T], ACT.Copy)\
                            .then_inc(emptied, 1)
                    if a and (s, u) == (0, 0):
                        copy_out(k, "A xT0", xnT[:, 0, :], sh_ps[:])
                    if a and (s, u) == (0, 1):
                        copy_out(k, "A xT1", xnT[:, 1, :], sh_ps[:])
                    if a and (s, u) == (0, 3):
                        copy_out(k, "A down", downT[:], sh_ps[:])
                    if a and (s, u) == (0, 4):
                        hi(k, 0)
                    if a and s == 1 and u < 2:
                        mid(k, u)
                        hi(k, u + 1)
                    if a and (s, u) == (1, 3):
                        mid(k, 3)
                    if a and s == 2 and u >= 3:
                        values(k, u - 3, 1 - par)
                    if d and (s, u) == (3, 1):
                        copy_out(k, "D xT0", xn2T[:, 0, :], sh_ps[:])
                    if d and (s, u) == (3, 4):
                        tanh(k, 0)
                        tanh(k, 1)

            def tail():
                outputs(NB, 1, 4 * NB + 1)
                copy_out(NB, "D xT0", xn2T[:, 0, :], sh_ps[:])
                copy_out(NB, "D xT1", xn2T[:, 1, :], sh_ps[:])
                tanh(NB, 0)
                tanh(NB, 1)

            programme(act, prelude, step, tail)

        @block.vector
        def _(dve):
            passed = dve_passed

            def prep(i, dst, src):
                dve.wait_ge(prep_mm, i + 1)
                nc.vector.tensor_copy(dst, src).then_inc(prep_out, 1)

            def statistics(src, tiles, st_, done):
                for t in tiles:
                    last = nc.vector.bn_stats(st_[:, t, :], src[:, t, :])
                if tiles[-1] == NT - 1:
                    last.then_inc(done, 1)

            def aggregate(b, st_, done, mean_var, ok):
                wait_apart(dve, done, b + 1, passed)
                for t in range(NT):
                    last = nc.vector.bn_aggr(mean_var[:, t, :], st_[:, t, :])
                last.then_inc(ok, 1)

            def stats1(b):
                dve.wait_ge(x_in, b * 16 + 16)
                wait(dve, xn_ok, b)
                statistics(xin, range(NT), stats, stat1)

            def left(k, j):
                which, g = j // 2, j % 2
                dve.wait_ge(hi_ok, k * 4 + (4 + j + 1))
                nc.vector.tensor_tensor(rest[which][g][:], sh_ps[:], part[which][0][:, g, :], ALU.subtract)\
                    .then_inc(emptied, 1)

            def unit(n, s, i):
                wait_apart(dve, s_full, n * UNITS + (i + 1), passed)
                for hh, t, at in unit_parts(i):
                    last = nc.vector.tensor_tensor_reduce(
                        scrap[:, i % 2, at:at + P * (t + 1)], s_ps[:, i % 2, at:at + P * (t + 1)],
                        causal[:, T - P * (t + 1):T], 1.0, MASKED, ALU.add, ALU.max,
                        mx[:, s, t, hh:hh + 1])
                last.then_inc(s_read, 1)

            def normalise(k, t):
                b = k - 1
                y = sh_ps[:].rearrange("p (h e) -> p h e", h=NH)
                dve.wait_ge(filled, fill_no(k, f"D y{t}") + 1)
                nc.vector.reciprocal(rden[:, t % 2, :], y[:, :, HS]).then_inc(rden_ok, 1)
                dve.wait_ge(rden_ok, b * NT + (t + 1))
                nc.vector.tensor_tensor(yb[:, t, :].rearrange("p (h d) -> p h d", h=NH), y[:, :, 0:HS],
                                        rden[:, t % 2, :].unsqueeze(2).to_broadcast([P, NH, HS]), ALU.mult)\
                    .then_inc(emptied, 1)

            def stats2_(b, tiles):
                dve.wait_ge(x1_ok, b * NT + (tiles[-1] + 1))
                statistics(x1, tiles, stats2, stat2)

            def add_bias(k, f):
                dve.wait_ge(filled, fill_no(k, f"D f{f}") + 1)
                nc.vector.tensor_tensor(hb[:, f], sh_ps[:].rearrange("p (t c) -> p t c", t=2), bias_b[:],
                                        ALU.add).then_inc(emptied, 1)

            def prelude():
                dve.wait_ge(consts, 1)
                prep(0, gqk[:], st_ps[0:L, 0, 0, 0:L])
                prep(1, wk[L:P, :], st_ps[L:P, 0, 1, 0:C])
                prep(2, wv[L:P, :], st_ps[L:P, 1, 0, 0:C])
                prep(3, m1T[:], st_ps[:, 1, 1, :].rearrange("p (t c) -> p t c", t=CT))
                prep(4, wf[:], s_ps[:, 0, :].rearrange("p (t c) -> p t c", t=CT))
                stats1(0)
                aggregate(0, stats, stat1, mv, mv1)
                for j in range(4):
                    left(-1, j)

            def step(k, s, par):
                _, _, ss = has(k, s)
                a, d = jobs(k)
                for u in range(PAIRS):
                    if ss:
                        for i in (2 * u, 2 * u + 1):
                            unit(k * 4 + (s + 1), (s + 1) % NQ, i)
                    if a and (s, u) == (0, 4):
                        left(k, 0)
                    if a and s == 1 and u < 3:
                        left(k, u + 1)
                    if d and (s, u) in Y_SLOTS:
                        normalise(k, Y_SLOTS.index((s, u)))
                    if d and (s, u) == (2, 2):
                        stats2_(k - 1, [0, 1])
                    if d and (s, u) == (2, 3):
                        stats2_(k - 1, [2, 3])
                        aggregate(k - 1, stats2, stat2, mv2, mv2_ok)
                    if (s, u) == (3, 1) and has_batch(k + 2):
                        stats1(k + 2)
                    if (s, u) == (3, 2) and has_batch(k + 2):
                        aggregate(k + 2, stats, stat1, mv, mv1)
                    if d and s == 3 and u >= 3:
                        add_bias(k, u - 3)

            def tail():
                for t in range(NT):
                    normalise(NB, t)
                stats2_(NB - 1, range(NT))
                aggregate(NB - 1, stats2, stat2, mv2, mv2_ok)
                add_bias(NB, 0)
                add_bias(NB, 1)

            programme(dve, prelude, step, tail)

        @block.tensor
        def _(pe):
            mm = nc.tensor.matmul

            def prelude():
                pe.wait_ge(w_in, 16 * N_W)
                pe.wait_ge(consts, 1)
                for c in range(CT):
                    last = mm(st_ps[0:L, 0, 0, 0:L], wuq[:, c, :], wuk[:, c, :], start=c == 0, stop=c == CT - 1)
                last.then_inc(prep_mm, 1)
                pe.wait_ge(prep_out, 1)
                mm(st_ps[L:P, 0, 1, 0:C], gqk[:], wdq[:], start=True, stop=True).then_inc(prep_mm, 1)
                for c in range(CT):
                    last = mm(st_ps[L:P, 1, 0, 0:C], wuv[:, c, :], woT[:, c, :], start=c == 0, stop=c == CT - 1)
                last.then_inc(prep_mm, 1)
                for m in range(CT):
                    for c in range(CT):
                        last = mm(st_ps[:, 1, 1, C * m:C * (m + 1)], wa1[:, c, P * m:P * (m + 1)], w1T[:, c, :],
                                  start=c == 0, stop=c == CT - 1)
                last.then_inc(prep_mm, 1)
                pe.wait_ge(prep_out, 4)
                for m in range(CT):
                    for c in range(CT):
                        last = mm(s_ps[:, 0, C * m:C * (m + 1)], m1T[:, c, P * m:P * (m + 1)], wa2[:, c, :],
                                  start=c == 0, stop=c == CT - 1)
                last.then_inc(prep_mm, 1)
                pe.wait_ge(prep_out, 5)
                for name in A_FILLS:
                    fill(-1, name, 0)

            def fill(k, name, s):
                wait(pe, emptied, fill_no(k, name))
                kind, i = name[:-1], int(name[-1]) if name[-1].isdigit() else 0
                if name[:3] == "A x":
                    if i == 0:
                        pe.wait_ge(xn_ok, k + 2)
                    for t in range(NT):
                        last = nc.tensor.transpose(sh_ps[:, P * t:P * (t + 1)], xn[:, t, P * i:P * (i + 1)],
                                                   ident[:])
                elif name == "A down":
                    for c in range(CT):
                        last = mm(sh_ps[:], wd[:, c, :], xnT[:, c, :], start=c == 0, stop=c == CT - 1)
                elif name[:3] == "A q":
                    w, g = (wq, wk)[i // 2], i % 2
                    last = mm(sh_ps[:], w[:, P * g:P * (g + 1)], downT[:], start=True, stop=True)
                elif name[:3] == "A v":
                    for t in range(2):
                        at = P * (2 * i + t)
                        last = mm(sh_ps[:, C * t:C * (t + 1)], downT[:, at:at + P], wv[:], start=True, stop=True)
                elif name[:1] == "M":
                    pe.wait_ge(neg, (k * 4 + s) * 5 + 5)
                    for t in range(NT):
                        last = nc.tensor.transpose(sh_bf[0:3 * HQ, P * t:P * (t + 1)],
                                                   nm[:, s % 2, t, :, :].rearrange("p i h -> p (i h)"), ident_b[:])
                elif name[:3] == "D y":
                    pe.wait_ge(yT_ok, k * 4)
                    for q in range(NQ):
                        last = nc.tensor.transpose(sh_ps[:, P * q:P * (q + 1)], yT[:, q, P * i:P * (i + 1)],
                                                   ident[:])
                elif name[:3] == "D x":
                    if i == 0:
                        pe.wait_ge(xn2_ok, k)
                    for t in range(NT):
                        last = nc.tensor.transpose(sh_ps[:, P * t:P * (t + 1)], xn2[:, t, P * i:P * (i + 1)],
                                                   ident[:])
                else:
                    for t in range(2):
                        at = P * (2 * i + t)
                        for c in range(CT):
                            last = mm(sh_ps[:, C * t:C * (t + 1)], xn2T[:, c, at:at + P], wf[:, c, :],
                                      start=c == 0, stop=c == CT - 1)
                last.then_inc(filled, 1)

            def transposed_scores(k, s, u, par):
                q, sp_, pair = (s - 1) % NQ, (1 - par if s == 0 else par), (k * 4 + (s - 1)) * PAIRS + u
                if u == 0:
                    pe.wait_ge(max_in[(s - 1) % 2], k * 32 + (16 * (s // 2 + 1) if s % 2 else 16 * (s // 2)))
                wait(pe, exp_ok, pair - 1)
                for bank in range(2):
                    to = st_ps[:, (s + 1 + u) % 2, bank, :]
                    at_diagonal, masks = {0: (to[:, 0:P], 1), 1: (to[:, 0:2 * P], 2), 2: (
                        to.rearrange("p (x y) -> p x y", x=2)[:, :, 0:P], 2)}[u // 2]
                    mm(at_diagonal, ident_b[:], after[:, 0:masks, :], start=True, stop=False,
                       skip_group_check=True)
                    for b_, at, hh, j in pair_parts(u):
                        if b_ == bank:
                            h = HQ * q + hh
                            last = mm(to[:, at:at + T - P * j], ks[sp_][:, h, P * j:P * (j + 1)],
                                      qs[sp_][:, h, P * j:T], start=False, stop=True, skip_group_check=True)
                last.then_inc(st_full, 1)

            def scores(k, s, i, par):
                q, sp_, n = (s + 1) % NQ, (1 - par if s == NQ - 1 else par), k * 4 + (s + 1)
                if q == 0 and i == 0:
                    pe.wait_ge(stacked, (k + 2) * (16 * 2 * PARTS))
                wait(pe, s_read, n * UNITS + (i - 1))
                for hh, t, at in unit_parts(i):
                    h = HQ * q + hh
                    last = mm(s_ps[:, i % 2, at:at + P * (t + 1)], qs[sp_][0:ROWS, h, P * t:P * (t + 1)],
                              ks[sp_][0:ROWS, h, 0:P * (t + 1)], start=True, stop=True)
                last.then_inc(s_full, 1)

            def outputs(k, s, lag, tiles, par):
                q, vp, n = (s - lag) % NQ, (1 - par if s < lag else par), k * 4 + (s - lag)
                u = {0: 1, 1: 3, 2: 4}[tiles[0]]
                pe.wait_ge(exp_ok, n * PAIRS + (u + 1))
                if tiles[0] == 0:
                    wait(pe, yT_ok, n)
                for j in tiles:
                    for hh in range(HQ):
                        u, bank, at = next((u, b_, a_) for u in range(PAIRS) for b_, a_, h_, j_ in pair_parts(u)
                                           if (h_, j_) == (hh, j))
                        last = mm(pv_ps[32 * hh:32 * (hh + 1), P * j:T], vv[vp][:, j, HQ * q + hh, :],
                                  probs[u][:, bank, at:at + T - P * j], start=j == 0, stop=j == 2,
                                  skip_group_check=True)
                last.then_inc(pv_ok, 1)

            def step(k, s, par):
                st, _, ss = has(k, s)
                for u in range(PAIRS):
                    if st:
                        transposed_scores(k, s, u, par)
                    if ss:
                        scores(k, s, 2 * u, par)
                    if u == 0 and has_pv(k, s):
                        outputs(k, s, 2, [1, 3], par)
                    if u == 1 and has_pv(k, s):
                        outputs(k, s, 2, [2], par)
                    if u == 3 and st:
                        outputs(k, s, 1, [0], par)
                    if ss:
                        scores(k, s, 2 * u + 1, par)
                    for name in step_fills(k, s, u):
                        fill(k, name, s)

            def tail():
                outputs(NB, 1, 2, [1, 3], 0)
                outputs(NB, 1, 2, [2], 0)
                for name in D_FILLS:
                    fill(NB, name, 0)

            programme(pe, prelude, step, tail)


def pair_parts(u):
    if u < 2:
        return [(b, 0, 2 * u + b, 0) for b in range(2)]
    if u < 4:
        return [(b, at, 2 * (u - 2) + b, j) for b in range(2) for at, j in ((0, 3), (P, 1))]
    return [(b, 2 * P * i, 2 * b + i, 2) for b in range(2) for i in range(2)]


def unit_parts(i):
    a, i = 2 * (i // 5), i % 5
    if i < 2:
        return [(a + i, 3, 0)]
    if i < 4:
        return [(a + i - 2, 2, 0), (a + i - 2, 0, 3 * P)]
    return [(a, 1, 0), (a + 1, 1, 2 * P)]


def kernel(L0_attn_x, L0_attn_W_dq, L0_attn_W_uq, L0_attn_W_dkv, L0_attn_W_uk, L0_attn_W_uv, L0_attn_W_o,
           L0_ffn_weight, L0_ffn_aux_weight1, L0_ffn_aux_weight2, L0_ffn_bias):
    import numpy as np
    import concourse.bacc as bacc
    from concourse.bass_utils import run_bass_kernel_spmd

    x, w_dq, w_uq, w_dkv, w_uk, w_uv, w_o, w1, a1, a2, bias = (np.asarray(a) for a in (
        L0_attn_x, L0_attn_W_dq, L0_attn_W_uq, L0_attn_W_dkv, L0_attn_W_uk, L0_attn_W_uv, L0_attn_W_o,
        L0_ffn_weight, L0_ffn_aux_weight1, L0_ffn_aux_weight2, L0_ffn_bias))
    lat, c = w_dq.shape

    def spread(w):
        return np.ascontiguousarray(w.reshape(lat, 8, 2, HS).transpose(0, 2, 3, 1).reshape(lat, c))

    arrays = {
        "x": x, "w_down": np.concatenate([w_dq, w_dkv]).T, "w_uq": w_uq, "w_uqT": spread(w_uq.T), "w_uk": w_uk,
        "w_dq": spread(w_dq), "w_uv": w_uv, "w_oT": w_o.T, "w_1T": w1.T, "w_a1": a1, "w_a2": a2, "bias": bias,
    }
    arrays = {name: np.ascontiguousarray(a) for name, a in arrays.items()}
    nc = bacc.Bacc("TRN2", target_bir_lowering=False, num_devices=1)
    args = [nc.dram_tensor(name, a.shape, mybir.dt.from_np(a.dtype), kind="ExternalInput").ap()
            for name, a in arrays.items()]
    out = nc.dram_tensor("out", x.shape, F32, kind="ExternalOutput").ap()
    block_kernel(nc, *args, out)
    r = run_bass_kernel_spmd(nc, [arrays], core_ids=[0])
    return r.results[0]["out"]
```

```python
from contextlib import ExitStack

import concourse.bass as bass
from concourse import mybir

F32 = mybir.dt.float32
BF16 = mybir.dt.bfloat16
ALU = mybir.AluOpType
ACT = mybir.ActivationFunctionType

P = 128
NH, HS = 16, 16
HQ = 4
NQ = NH // HQ
PARTS = 6
ROWS = PARTS * HS
K_ST = ROWS + 3
Q_PART = (0, 0, 1, 1, 0, 2)
K_PART = (0, 1, 0, 1, 2, 0)
PAIRS = 5
UNITS = 9
HALF = P // 2
EPS = 1e-5
MASKED = -3.0e38

FILLS = (
    (0, 0, "A xT0"), (0, 1, "A xT1"), (0, 2, "A down"), (0, 3, "M 0"), (0, 3, "A qk0"), (0, 4, "A qk1"),
    (1, 0, "A qk2"), (1, 1, "A qk3"), (1, 2, "A v0"), (1, 3, "M 1"), (1, 3, "D y0"), (1, 4, "D y1"),
    (2, 0, "D y2"), (2, 1, "D y3"), (2, 2, "M 2"), (2, 3, "A v1"),
    (3, 1, "D xT0"), (3, 2, "D xT1"), (3, 3, "M 3"), (3, 3, "D f0"), (3, 4, "D f1"),
)
SPLIT_SLOTS = [(0, 4), (1, 0), (1, 1), (1, 2)]
MID_SLOTS = [(1, 0), (1, 1), (1, 2), (1, 3)]
LOW_SLOTS = [(1, 0), (1, 1), (1, 2), (1, 3)]
Y_SLOTS = [f[:2] for f in FILLS if f[2][:3] == "D y"]
A_FILLS = [f[2] for f in FILLS if f[2][0] == "A"]
D_FILLS = [f[2] for f in FILLS if f[2][0] == "D"]


def block_kernel(nc, x, w_down, w_uq, w_uqT, w_uk, w_dq, w_uv, w_oT, w_1T, w_a1, w_a2, bias, out):
    NB, T, C = x.shape
    NT = T // P
    CT = C // P
    L = w_uk.shape[1]
    SCALE = float(HS) ** -0.5
    assert (NT, CT, L) == (4, 2, 64)

    def known(k):
        return isinstance(k, int)

    def fills(k):
        return [f[2] for f in FILLS if not (f[2][0] == "A" and known(k) and k == NB - 1)
                and not (f[2][0] == "D" and known(k) and k == 0)]

    def fill_no(k, name):
        if known(k) and k == -1:
            return A_FILLS.index(name)
        base = len(A_FILLS)
        if known(k) and k == 0:
            return base + fills(0).index(name)
        base += len(fills(0))
        if known(k) and k == NB:
            return base + len(FILLS) * (NB - 2) + len(fills(NB - 1)) + D_FILLS.index(name)
        return (k - 1) * len(FILLS) + base + fills(k).index(name)

    def second_bank(k, name):
        return (known(k) and (k == -1 and A_FILLS.index(name) % 2 == 1
                              or k == NB and D_FILLS.index(name) % 2 == 1))

    def wait(eng, sem, value):
        if not known(value) or value > 0:
            eng.wait_ge(sem, value)

    def wait_apart(eng, sem, value, passed):
        eng.wait_ge(sem, value)
        if not known(value):
            eng.sem_inc(passed, 1)

    with ExitStack() as ctx:
        def sb(name, shape, dt=F32):
            return ctx.enter_context(nc.sbuf_tensor(name, shape, dt))

        def pb(name, shape, dt=F32):
            return ctx.enter_context(nc.psum_tensor(name, shape, dt))

        def sem(name):
            return ctx.enter_context(nc.semaphore(name))

        wd = sb("wd", [P, CT, P])
        wuq = sb("wuq", [P, CT, L])
        wuk = sb("wuk", [P, CT, L])
        wdq = sb("wdq", [L, C])
        wuv = sb("wuv", [P, CT, L])
        woT = sb("woT", [P, CT, C])
        w1T = sb("w1T", [P, CT, C])
        wa1 = sb("wa1", [P, CT, C])
        wa2 = sb("wa2", [P, CT, C])
        gqk = sb("gqk", [L, L])
        m1T = sb("m1T", [P, CT, C])
        wf = sb("wf", [P, CT, C])
        wq = sb("wq", [P, C])
        wk = sb("wk", [P, C])
        wv = sb("wv", [P, C])
        bias_b = sb("bias_b", [P, 2, C])
        ident = sb("ident", [P, P])
        ident_b = sb("ident_b", [P, P], BF16)
        causal = sb("causal", [P, T])
        after = sb("after", [P, 2, P], BF16)
        ones = sb("ones", [ROWS, NH * T * 3 // ROWS], BF16)
        half = sb("half", [P, NT])
        xin = sb("xin", [P, NT, C])
        xres = sb("xres", [P, NT, C])
        stats = sb("stats", [P, NT, 6])
        mv = sb("mv", [P, NT, 2])
        ve = sb("ve", [P, NT])
        rstd = sb("rstd", [P, NT])
        shift = sb("shift", [P, NT])
        nshift = sb("nshift", [P, NT])
        xn = sb("xn", [P, NT, C])
        xnT = sb("xnT", [P, CT, T])
        downT = sb("downT", [P, T])
        qk = [sb(f"qk{j}", [P, T]) for j in range(4)]
        qpart = [sb(f"qpart{i}", [P, T // HALF, 2, HALF], BF16) for i in range(3)]
        kpart = [sb(f"kpart{i}", [P, 2, T], BF16) for i in range(3)]
        rest = [[sb(f"{n}rest{g}", [P, T]) for g in range(2)] for n in "qk"]
        qs = [sb(f"qs{i}", [P, NH // 2, T // HALF, 2, HALF], BF16) for i in range(2)]
        ks = [sb(f"ks{i}", [P, NH, T], BF16) for i in range(2)]
        vv = [sb(f"vv{i}", [P, NT, NH, 32]) for i in range(2)]
        NM = HQ // 2 * (T // HALF)
        mx = sb("mx", [P, NQ, NM])
        scrap = sb("scrap", [P, 2, T], BF16)
        nm = sb("nm", [P, 2, 3, NM], BF16)
        nr = sb("nr", [P, 2, 2, NM])
        nmT = sb("nmT", [3 * NM, 2, P], BF16)
        probs = [sb(f"probs{u}", [P, 2, T]) for u in range(PAIRS)]
        yT = sb("yT", [P, NQ, T])
        rden = sb("rden", [P, 2, NH])
        yb = sb("yb", [P, NT, C])
        x1 = sb("x1", [P, NT, C])
        stats2 = sb("stats2", [P, NT, 6])
        mv2 = sb("mv2", [P, NT, 2])
        ve2 = sb("ve2", [P, NT])
        rstd2 = sb("rstd2", [P, NT])
        shift2 = sb("shift2", [P, NT])
        nshift2 = sb("nshift2", [P, NT])
        xn2 = sb("xn2", [P, NT, C])
        xn2T = sb("xn2T", [P, CT, T])
        hb = sb("hb", [P, 2, 2, C])
        xo = sb("xo", [P, 2, 2, C])

        st_ps = pb("st_ps", [P, 2, 2, T])
        s_ps = pb("s_ps", [P, 2, T])
        pv_ps = pb("pv_ps", [P, T])
        sh_ps = pb("sh_ps", [P, T])
        sh_bf = sh_ps[:].bitcast(BF16)

        w_in = sem("w_in")
        f_in = sem("f_in")
        dve_passed = sem("dve_passed")
        pool_passed = sem("pool_passed")
        pe_passed = sem("pe_passed")
        consts = sem("consts")
        tri0 = sem("tri0")
        padded = sem("padded")
        ones_in = sem("ones_in")
        prep_mm = sem("prep_mm")
        prep_out = sem("prep_out")
        x_in = sem("x_in")
        r_in = sem("r_in")
        stat1, mv1 = sem("stat1"), sem("mv1")
        pool1 = sem("pool1")
        xn_ok = sem("xn_ok")
        filled = sem("filled")
        emptied = sem("emptied")
        hi_ok = sem("hi_ok")
        rest_ok = sem("rest_ok")
        mid_ok = sem("mid_ok")
        low_ok = sem("low_ok")
        stacked = sem("stacked")
        s_full = sem("s_full")
        s_read = sem("s_read")
        neg = sem("neg")
        max_in = [sem(f"max_in{i}") for i in range(2)]
        st_full = sem("st_full")
        exp_ok = sem("exp_ok")
        pv_ok = sem("pv_ok")
        yT_ok = sem("yT_ok")
        rden_ok = sem("rden_ok")
        x1_ok = sem("x1_ok")
        stat2, mv2_ok = sem("stat2"), sem("mv2_ok")
        pool2 = sem("pool2")
        xn2_ok = sem("xn2_ok")
        th_ok = sem("th_ok")
        xo_ok = sem("xo_ok")
        xo_out = [sem(f"xo_out{i}") for i in range(2)]
        N_W, N_F = 7, 5

        block = ctx.enter_context(nc.Block())

        def programme(eng, prelude, step, tail):
            prelude()
            step(-1, 3, 1)
            for s in range(4):
                step(0, s, 0)
            with eng.Fori(0, (NB - 4) // 2) as i:
                for odd in range(2):
                    for s in range(4):
                        step(i * 2 + 1 + odd, s, 1 - odd)
            for k in range(NB - 3, NB):
                for s in range(4):
                    step(k, s, k % 2)
            step(NB, 0, 0)
            tail()

        def has(k, s):
            if not known(k):
                return True, True, True
            n = 4 * k + s
            return 0 <= n - 1 < NQ * NB, 0 <= n < NQ * NB, 0 <= n + 1 < NQ * NB

        def has_pv(k, s):
            return not known(k) or 0 <= 4 * k + s - 2 < NQ * NB

        def has_batch(b):
            return not known(b) or 0 <= b < NB

        def jobs(k):
            if not known(k):
                return True, True
            return 0 <= k < NB - 1, 1 <= k < NB

        def step_fills(k, s, u):
            if known(k) and k in (-1, NB):
                return []
            return [f[2] for f in FILLS if f[:2] == (s, u) and f[2] in fills(k)]

        def bank(k, name):
            return pv_ps if second_bank(k, name) else sh_ps

        def part(which, i, g):
            return (qpart[i][:, :, g, :], kpart[i][:, g, :])[which]

        def as_part(which, v):
            return (v.rearrange("p (j q) -> p j q", q=HALF), v)[which]

        @block.sync
        def _(sp):
            def load_x(b):
                wait(sp, xn_ok, b)
                sp.dma_start(xin[:], x[b].rearrange("(t p) c -> p t c", p=P)).then_inc(x_in, 16)

            def load_res(b):
                sp.dma_start(xres[:], x[b].rearrange("(t p) c -> p t c", p=P)).then_inc(r_in, 16)

            def stack_parts(b, par, which):
                stack, order = ((qs, Q_PART), (ks, K_PART))[which]
                if which == 0:
                    wait(sp, st_full, (b - 1) * (PAIRS * NQ))
                for r, p in sorted(enumerate(order), key=lambda a: a[1]):
                    sp.wait_ge((hi_ok, mid_ok, low_ok)[p], b * 4 + 2 * (which + 1))
                    sp.dma_start(stack[par][HS * r:HS * (r + 1)], (qpart, kpart)[which][p][:])\
                        .then_inc(stacked, 16)

            def max_rows(k, s, par):
                sp.wait_ge(emptied, fill_no(k, f"M {s}") + 1)
                sp.dma_start(qs[par][ROWS:ROWS + 3, 2 * s:2 * (s + 1)], nmT[:, s % 2, :])\
                    .then_inc(max_in[s % 2], 16)

            def store(b, f):
                sp.wait_ge(xo_ok, b * 2 + (f + 1))
                sp.dma_start(out[b, 2 * f * P:2 * (f + 1) * P, :].rearrange("(t p) c -> p t c", p=P),
                             xo[:, f]).then_inc(xo_out[f], 16)

            def prelude():
                load_x(0)
                for dst, src in ((wuq, w_uq), (wuk, w_uk), (wuv, w_uv), (woT, w_oT), (wd, w_down)):
                    sp.dma_start(dst[:], src.rearrange("(t p) n -> p t n", p=P)).then_inc(w_in, 16)
                sp.dma_start(wdq[:], w_dq).then_inc(w_in, 16)
                sp.wait_ge(consts, 1)
                sp.dma_start(wq[0:L, :], w_uqT).then_inc(w_in, 16)
                for dst, src in ((w1T, w_1T), (wa1, w_a1), (wa2, w_a2)):
                    sp.dma_start(dst[:], src.rearrange("(t p) n -> p t n", p=P)).then_inc(f_in, 16)
                for t in range(2):
                    sp.dma_start(bias_b[:, t, :], bias.partition_broadcast(P)).then_inc(f_in, 16)
                sp.wait_ge(padded, 1)
                for i in range(2):
                    sp.dma_start(ks[i][ROWS:K_ST], ones[:]).then_inc(ones_in, 16)
                load_x(1)
                stack_parts(0, 0, 0)
                stack_parts(0, 0, 1)

            def step(k, s, par):
                _, mt, _ = has(k, s)
                a, d = jobs(k)
                if s == 0 and mt:
                    if has_batch(k + 2):
                        load_x(k + 2)
                    if d:
                        load_res(k - 1)
                if s == 1 and a:
                    stack_parts(k + 1, 1 - par, 0)
                if mt:
                    max_rows(k, s, par)
                if s == 1 and a:
                    stack_parts(k + 1, 1 - par, 1)
                if s == 3 and d:
                    store(k - 1, 0)
                    store(k - 1, 1)

            def tail():
                load_res(NB - 1)
                store(NB - 1, 0)
                store(NB - 1, 1)
                for f in range(2):
                    sp.wait_ge(xo_out[f], 16 + 16 * NB)

            programme(sp, prelude, step, tail)

        @block.gpsimd
        def _(pool):
            passed = pool_passed

            def prelude():
                for t in (wk, wv, wq, ident, ident_b, causal, after):
                    nc.gpsimd.memset(t[:], 0.0)
                nc.gpsimd.memset(half[:], -0.5).then_inc(tri0, 1)
                pool.wait_ge(tri0, 1)
                for t in (ident, ident_b):
                    nc.gpsimd.affine_select(out=t[:], in_=t[:], compare_op=ALU.not_equal, fill=1.0, base=0,
                                            pattern=[[-1, P]], channel_multiplier=1)
                nc.gpsimd.affine_select(out=after[:], in_=after[:], compare_op=ALU.is_ge, fill=MASKED, base=0,
                                        pattern=[[0, 2], [1, P]], channel_multiplier=-1).then_inc(tri0, 1)
                for a in range(2):
                    tri = causal[HALF * a:HALF * (a + 1), T - HALF:T]
                    pool.wait_ge(tri0, 2 + a)
                    nc.gpsimd.affine_select(out=tri, in_=tri, compare_op=ALU.is_ge, fill=MASKED, base=0,
                                            pattern=[[-1, HALF]], channel_multiplier=1)\
                        .then_inc((tri0, consts)[a], 1)
                pool.wait_ge(consts, 1)
                norm1(0)
                for f in range(2):
                    pool.sem_inc(xo_out[f], 16)
                norm1(1)

            def norm(b, src, into, mean_var, done, chain, ok, tmp):
                ve_, rstd_, shift_, nshift_ = tmp
                wait_apart(pool, done, b + 1, passed)
                nc.gpsimd.tensor_scalar(ve_[:], mean_var[:, :, 1], 1.0, EPS, ALU.mult, ALU.add)\
                    .then_inc(chain, 1)
                pool.wait_ge(chain, b * 4 + 1)
                nc.gpsimd.tensor_tensor(rstd_[:], ve_[:], half[:], ALU.pow).then_inc(chain, 1)
                pool.wait_ge(chain, b * 4 + 2)
                nc.gpsimd.tensor_tensor(shift_[:], mean_var[:, :, 0], rstd_[:], ALU.mult).then_inc(chain, 1)
                wait_apart(pool, chain, b * 4 + 3, passed)
                nc.gpsimd.tensor_scalar(nshift_[:], shift_[:], -1.0, 1.0, ALU.mult, ALU.mult)\
                    .then_inc(chain, 1)
                wait_apart(pool, chain, b * 4 + 4, passed)
                for t in range(NT):
                    last = nc.gpsimd.tensor_scalar(into[:, t, :], src[:, t, :], rstd_[:, t:t + 1],
                                                   nshift_[:, t:t + 1], ALU.mult, ALU.add)
                last.then_inc(ok, 1)

            def norm1(b):
                norm(b, xin, xn, mv, mv1, pool1, xn_ok, (ve, rstd, shift, nshift))

            def norm2(b):
                norm(b, x1, xn2, mv2, mv2_ok, pool2, xn2_ok, (ve2, rstd2, shift2, nshift2))

            def low(b, j):
                which, g = j // 2, j % 2
                pool.wait_ge(mid_ok, b * 4 + (j + 1))
                nc.gpsimd.tensor_tensor(part(which, 2, g), as_part(which, rest[which][g][:]), part(which, 1, g),
                                        ALU.subtract).then_inc(low_ok, 1)

            def negate(n, s):
                i = s % 2
                m = mx[:, s, :]
                wait_apart(pool, s_read, n * UNITS + UNITS, passed)
                nc.gpsimd.tensor_scalar(nm[:, i, 0], m, -1.0, 1.0, ALU.mult, ALU.mult).then_inc(neg, 1)
                pool.wait_ge(neg, n * 5 + 1)
                nc.gpsimd.tensor_tensor(nr[:, i, 0], m, nm[:, i, 0], ALU.add).then_inc(neg, 1)
                wait_apart(pool, neg, n * 5 + 2, passed)
                nc.gpsimd.tensor_scalar(nm[:, i, 1], nr[:, i, 0], -1.0, 1.0, ALU.mult, ALU.mult)\
                    .then_inc(neg, 1)
                pool.wait_ge(neg, n * 5 + 3)
                nc.gpsimd.tensor_tensor(nr[:, i, 1], nr[:, i, 0], nm[:, i, 1], ALU.add).then_inc(neg, 1)
                wait_apart(pool, neg, n * 5 + 4, passed)
                nc.gpsimd.tensor_scalar(nm[:, i, 2], nr[:, i, 1], -1.0, 1.0, ALU.mult, ALU.mult)\
                    .then_inc(neg, 1)

            def add_residual(k, t):
                b = k - 1
                pool.wait_ge(emptied, fill_no(k, f"D y{t}") + 1)
                if t == 0:
                    pool.wait_ge(r_in, b * 16 + 16)
                nc.gpsimd.tensor_tensor(x1[:, t, :], yb[:, t, :], xres[:, t, :], ALU.add)\
                    .then_inc(x1_ok, 1)

            def add_ffn(b, f):
                pool.wait_ge(th_ok, b * 2 + (f + 1))
                pool.wait_ge(xo_out[f], b * 16 + 16)
                nc.gpsimd.tensor_tensor(xo[:, f], x1[:, 2 * f:2 * f + 2, :], hb[:, f], ALU.add)\
                    .then_inc(xo_ok, 1)

            def step(k, s, par):
                st, mt, _ = has(k, s)
                a, d = jobs(k)
                n = k * 4 + s
                for u in range(PAIRS):
                    if u == 0 and mt:
                        negate(n, s)
                    if a and (s, u) in LOW_SLOTS:
                        low(k + 1, LOW_SLOTS.index((s, u)))
                    if d and (s, u) in Y_SLOTS:
                        add_residual(k, Y_SLOTS.index((s, u)))
                    if d and (s, u) == (2, 2):
                        norm2(k - 1)
                    if st and (s, u) == (3, 3) and has_batch(k + 2):
                        norm1(k + 2)
                    if d and (s, u) == (3, 4):
                        add_ffn(k - 1, 0)
                        add_ffn(k - 1, 1)

            def tail():
                for t in range(NT):
                    add_residual(NB, t)
                norm2(NB - 1)
                add_ffn(NB - 1, 0)
                add_ffn(NB - 1, 1)

            programme(pool, prelude, step, tail)

        @block.scalar
        def _(act):
            def copy_out(k, name, dst, view=lambda whole: whole):
                act.wait_ge(filled, fill_no(k, name) + 1)
                nc.scalar.activation(dst, view(bank(k, name)[:]), ACT.Copy).then_inc(emptied, 1)

            def mid(k, j):
                which, g = j // 2, j % 2
                act.wait_ge(rest_ok, k * 4 + (4 + j + 1))
                nc.scalar.activation(part(which, 1, g), as_part(which, rest[which][g][:]), ACT.Copy)\
                    .then_inc(mid_ok, 1)

            def values(k, f, par):
                copy_out(k, f"A v{f}", vv[par][:, 2 * f:2 * f + 2, :, 0:HS],
                         lambda whole: whole.rearrange("p (t h d) -> p t h d", t=2, h=NH))

            def prelude():
                copy_out(-1, "A xT0", xnT[:, 0, :])
                copy_out(-1, "A xT1", xnT[:, 1, :])
                copy_out(-1, "A down", downT[:])
                for j in range(4):
                    copy_out(-1, f"A qk{j}", qk[j][:])
                    if j > 0:
                        mid(-1, j - 1)
                mid(-1, 3)
                act.wait_ge(padded, 1)
                values(-1, 0, 0)
                values(-1, 1, 0)

            def exp(n, s, u):
                pair = (n - 1) * PAIRS + u
                act.wait_ge(st_full, pair + 1)
                wait(act, pv_ok, (n - 2) * 3 + (1, 1, 2, 2, 3)[u])
                nc.scalar.activation(probs[u][:], st_ps[:, (s + 1 + u) % 2, :, :], ACT.Exp, scale=SCALE)\
                    .then_inc(exp_ok, 1)

            def outputs(k, s, n):
                act.wait_ge(pv_ok, (n - 2) * 3 + 3)
                if s == 2 and jobs(k)[1]:
                    act.wait_ge(filled, fill_no(k, "D y3") + 1)
                nc.scalar.activation(yT[:, (s - 2) % NQ, :], pv_ps[:], ACT.Copy).then_inc(yT_ok, 1)

            def tanh(k, f):
                act.wait_ge(emptied, fill_no(k, f"D f{f}") + 1)
                nc.scalar.activation(hb[:, f], hb[:, f], ACT.Tanh).then_inc(th_ok, 1)

            def evacuate(k, name, s, par):
                i = int(name[-1]) if name[-1].isdigit() else 0
                if name[:3] == "A x":
                    copy_out(k, name, xnT[:, i, :])
                elif name == "A down":
                    copy_out(k, name, downT[:])
                elif name[:3] == "A q":
                    copy_out(k, name, qk[i][:])
                elif name[:3] == "A v":
                    values(k, i, 1 - par)
                elif name[0] == "M":
                    copy_out(k, name, nmT[:, s % 2, :], lambda whole: sh_bf[0:3 * NM, 0:P])
                elif name[:3] == "D x":
                    copy_out(k, name, xn2T[:, i, :])

            def step(k, s, par):
                st, _, _ = has(k, s)
                a, d = jobs(k)
                n = k * 4 + s
                for u in range(PAIRS):
                    if st:
                        exp(n, s, u)
                    if u == 1 and has_pv(k, s):
                        outputs(k, s, n)
                    for name in step_fills(k, s, u):
                        evacuate(k, name, s, par)
                    if a and (s, u) in MID_SLOTS:
                        mid(k, MID_SLOTS.index((s, u)))
                    if d and (s, u) == (3, 4):
                        tanh(k, 0)
                        tanh(k, 1)

            def tail():
                outputs(NB, 1, 4 * NB + 1)
                copy_out(NB, "D xT0", xn2T[:, 0, :])
                copy_out(NB, "D xT1", xn2T[:, 1, :])
                tanh(NB, 0)
                tanh(NB, 1)

            programme(act, prelude, step, tail)

        @block.vector
        def _(dve):
            passed = dve_passed

            def prep(i, dst, src):
                dve.wait_ge(prep_mm, i + 1)
                nc.vector.tensor_copy(dst, src).then_inc(prep_out, 1)

            def statistics(src, tiles, st_, done):
                for t in tiles:
                    last = nc.vector.bn_stats(st_[:, t, :], src[:, t, :])
                if tiles[-1] == NT - 1:
                    last.then_inc(done, 1)

            def aggregate(b, st_, done, mean_var, ok):
                wait_apart(dve, done, b + 1, passed)
                for t in range(NT):
                    last = nc.vector.bn_aggr(mean_var[:, t, :], st_[:, t, :])
                last.then_inc(ok, 1)

            def stats1(b, tiles):
                if tiles[0] == 0:
                    dve.wait_ge(x_in, b * 16 + 16)
                    wait(dve, xn_ok, b)
                statistics(xin, tiles, stats, stat1)

            def split(k, j):
                which, g = j // 2, j % 2
                dve.wait_ge(emptied, fill_no(k, f"A qk{j}") + 1)
                if j == 0:
                    wait(dve, stacked, (k + 1) * (16 * 2 * PARTS))
                nc.vector.tensor_copy(part(which, 0, g), as_part(which, qk[j][:])).then_inc(hi_ok, 1)
                dve.wait_ge(hi_ok, k * 4 + (4 + j + 1))
                nc.vector.tensor_tensor(as_part(which, rest[which][g][:]), as_part(which, qk[j][:]),
                                        part(which, 0, g), ALU.subtract).then_inc(rest_ok, 1)

            def low0(j):
                which, g = j // 2, j % 2
                dve.wait_ge(mid_ok, j + 1)
                nc.vector.tensor_tensor(part(which, 2, g), as_part(which, rest[which][g][:]), part(which, 1, g),
                                        ALU.subtract).then_inc(low_ok, 1)

            def unit(n, s, i):
                wait_apart(dve, s_full, n * UNITS + (i + 1), passed)
                bank = (s + i) % 2
                for pair, j, at in unit_parts(i):
                    w = HALF * (j + 1)
                    last = nc.vector.tensor_tensor_reduce(
                        scrap[:, bank, at:at + w], s_ps[:, bank, at:at + w], causal[:, T - w:T], 1.0, MASKED,
                        ALU.add, ALU.max, mx[:, s, T // HALF * pair + j:T // HALF * pair + j + 1])
                last.then_inc(s_read, 1)

            def normalise(k, t):
                b = k - 1
                y = bank(k, f"D y{t}")[:].rearrange("p (h e) -> p h e", h=NH)
                dve.wait_ge(filled, fill_no(k, f"D y{t}") + 1)
                nc.vector.reciprocal(rden[:, t % 2, :], y[:, :, HS]).then_inc(rden_ok, 1)
                dve.wait_ge(rden_ok, b * NT + (t + 1))
                nc.vector.tensor_tensor(yb[:, t, :].rearrange("p (h d) -> p h d", h=NH), y[:, :, 0:HS],
                                        rden[:, t % 2, :].unsqueeze(2).to_broadcast([P, NH, HS]), ALU.mult)\
                    .then_inc(emptied, 1)

            def stats2_(b, tiles):
                dve.wait_ge(x1_ok, b * NT + (tiles[-1] + 1))
                statistics(x1, tiles, stats2, stat2)

            def add_bias(k, f):
                dve.wait_ge(filled, fill_no(k, f"D f{f}") + 1)
                nc.vector.tensor_tensor(hb[:, f], bank(k, f"D f{f}")[:].rearrange("p (t c) -> p t c", t=2),
                                        bias_b[:], ALU.add).then_inc(emptied, 1)

            def prelude():
                for i in range(2):
                    nc.vector.memset(vv[i][:, :, :, HS:HS + 1], 1.0)
                    nc.vector.memset(vv[i][:, :, :, HS + 1:], 0.0)
                nc.vector.memset(ones[:], 1.0).then_inc(padded, 1)
                stats1(0, range(NT))
                aggregate(0, stats, stat1, mv, mv1)
                dve.wait_ge(consts, 1)
                prep(0, gqk[:], st_ps[0:L, 0, 0, 0:L])
                prep(1, wk[L:P, :], st_ps[L:P, 0, 1, 0:C])
                prep(2, wv[L:P, :], st_ps[L:P, 1, 0, 0:C])
                prep(3, m1T[:], st_ps[:, 1, 1, :].rearrange("p (t c) -> p t c", t=CT))
                for j in range(4):
                    split(-1, j)
                    if j > 0:
                        low0(j - 1)
                low0(3)
                prep(4, wf[:], s_ps[:, 0, :].rearrange("p (t c) -> p t c", t=CT))
                stats1(1, range(NT))
                aggregate(1, stats, stat1, mv, mv1)

            def step(k, s, par):
                _, _, ss = has(k, s)
                a, d = jobs(k)
                for u in range(PAIRS):
                    if ss:
                        for i in range(2 * u, min(2 * u + 2, UNITS)):
                            unit(k * 4 + (s + 1), (s + 1) % NQ, i)
                    if a and (s, u) in SPLIT_SLOTS:
                        split(k, SPLIT_SLOTS.index((s, u)))
                    for name in step_fills(k, s, u):
                        i = int(name[-1]) if name[-1].isdigit() else 0
                        if name[:3] == "D y":
                            normalise(k, i)
                        elif name[:3] == "D f":
                            add_bias(k, i)
                    if d and (s, u) == (2, 1):
                        stats2_(k - 1, [0, 1])
                    if d and (s, u) == (2, 2):
                        stats2_(k - 1, [2, 3])
                        aggregate(k - 1, stats2, stat2, mv2, mv2_ok)
                    if has(k, s)[0] and (s, u) == (2, 4) and has_batch(k + 2):
                        stats1(k + 2, [0, 1])
                    if has(k, s)[0] and (s, u) == (3, 1) and has_batch(k + 2):
                        stats1(k + 2, [2, 3])
                    if has(k, s)[0] and (s, u) == (3, 2) and has_batch(k + 2):
                        aggregate(k + 2, stats, stat1, mv, mv1)

            def tail():
                for t in range(NT):
                    normalise(NB, t)
                    if t == 2:
                        stats2_(NB - 1, [0, 1])
                stats2_(NB - 1, [2, 3])
                aggregate(NB - 1, stats2, stat2, mv2, mv2_ok)
                add_bias(NB, 0)
                add_bias(NB, 1)

            programme(dve, prelude, step, tail)

        @block.tensor
        def _(pe):
            mm = nc.tensor.matmul

            def prelude():
                pe.wait_ge(w_in, 16 * N_W)
                pe.wait_ge(consts, 1)
                for c in range(CT):
                    last = mm(st_ps[0:L, 0, 0, 0:L], wuq[:, c, :], wuk[:, c, :], start=c == 0, stop=c == CT - 1)
                last.then_inc(prep_mm, 1)
                pe.wait_ge(prep_out, 1)
                mm(st_ps[L:P, 0, 1, 0:C], gqk[:], wdq[:], start=True, stop=True).then_inc(prep_mm, 1)
                for c in range(CT):
                    last = mm(st_ps[L:P, 1, 0, 0:C], wuv[:, c, :], woT[:, c, :], start=c == 0, stop=c == CT - 1)
                last.then_inc(prep_mm, 1)
                pe.wait_ge(prep_out, 3)
                for name in A_FILLS[:3]:
                    fill(-1, name, 0)
                pe.wait_ge(f_in, 16 * N_F)
                for m in range(CT):
                    for c in range(CT):
                        last = mm(st_ps[:, 1, 1, C * m:C * (m + 1)], wa1[:, c, P * m:P * (m + 1)], w1T[:, c, :],
                                  start=c == 0, stop=c == CT - 1)
                last.then_inc(prep_mm, 1)
                for name in A_FILLS[3:]:
                    fill(-1, name, 0)
                pe.wait_ge(prep_out, 4)
                for m in range(CT):
                    for c in range(CT):
                        last = mm(s_ps[:, 0, C * m:C * (m + 1)], m1T[:, c, P * m:P * (m + 1)], wa2[:, c, :],
                                  start=c == 0, stop=c == CT - 1)
                last.then_inc(prep_mm, 1)
                pe.wait_ge(prep_out, 5)
                pe.wait_ge(ones_in, 32)

            def fill(k, name, s):
                no = fill_no(k, name)
                if known(k) and k in (-1, NB) and name not in ("A down", "A qk0", "D f0"):
                    no -= 1
                wait(pe, emptied, no)
                to = bank(k, name)
                i = int(name[-1]) if name[-1].isdigit() else 0
                if name[:3] == "A x":
                    if i == 0:
                        pe.wait_ge(xn_ok, k + 2)
                    for t in range(NT):
                        last = nc.tensor.transpose(to[:, P * t:P * (t + 1)], xn[:, t, P * i:P * (i + 1)],
                                                   ident[:])
                elif name == "A down":
                    for c in range(CT):
                        last = mm(to[:], wd[:, c, :], xnT[:, c, :], start=c == 0, stop=c == CT - 1)
                elif name[:3] == "A q":
                    w, g = (wq, wk)[i // 2], i % 2
                    last = mm(to[:], w[:, P * g:P * (g + 1)], downT[:], start=True, stop=True)
                elif name[:3] == "A v":
                    for t in range(2):
                        at = P * (2 * i + t)
                        last = mm(to[:, C * t:C * (t + 1)], downT[:, at:at + P], wv[:], start=True, stop=True)
                elif name[:1] == "M":
                    wait_apart(pe, neg, (k * 4 + s) * 5 + 5, pe_passed)
                    last = nc.tensor.transpose(sh_bf[0:3 * NM, 0:P],
                                               nm[:, s % 2].rearrange("p i m -> p (i m)"), ident_b[:])
                elif name[:3] == "D y":
                    pe.wait_ge(yT_ok, k * 4)
                    for q in range(NQ):
                        last = nc.tensor.transpose(to[:, P * q:P * (q + 1)], yT[:, q, P * i:P * (i + 1)],
                                                   ident[:])
                elif name[:3] == "D x":
                    if i == 0:
                        pe.wait_ge(xn2_ok, k)
                    for t in range(NT):
                        last = nc.tensor.transpose(to[:, P * t:P * (t + 1)], xn2[:, t, P * i:P * (i + 1)],
                                                   ident[:])
                else:
                    for t in range(2):
                        at = P * (2 * i + t)
                        for c in range(CT):
                            last = mm(to[:, C * t:C * (t + 1)], xn2T[:, c, at:at + P], wf[:, c, :],
                                      start=c == 0, stop=c == CT - 1)
                last.then_inc(filled, 1)

            def transposed_scores(k, s, u, par):
                q, sp_, pair = (s - 1) % NQ, (1 - par if s == 0 else par), (k * 4 + (s - 1)) * PAIRS + u
                if u == 0:
                    pe.wait_ge(max_in[(s - 1) % 2], k * 32 + (16 * (s // 2 + 1) if s % 2 else 16 * (s // 2)))
                wait(pe, exp_ok, pair - 1)
                for bank in range(2):
                    to = st_ps[:, (s + 1 + u) % 2, bank, :]
                    at_diagonal, masks = {0: (to[:, 0:P], 1), 1: (to[:, 0:2 * P], 2), 2: (
                        to.rearrange("p (x y) -> p x y", x=2)[:, :, 0:P], 2)}[u // 2]
                    mm(at_diagonal, ident_b[:], after[:, 0:masks, :], start=True, stop=False,
                       skip_group_check=True)
                    for b_, at, hh, j in pair_parts(u):
                        if b_ == bank:
                            h = HQ * q + hh
                            last = mm(to[:, at:at + T - P * j].rearrange("p (x y) -> p x y", y=HALF),
                                      ks[sp_][0:K_ST, h, P * j:P * (j + 1)], qs[sp_][0:K_ST, h // 2, 2 * j:, h % 2, :],
                                      start=False, stop=True, skip_group_check=True)
                last.then_inc(st_full, 1)

            def scores(k, s, i, par):
                q, sp_, n = (s + 1) % NQ, (1 - par if s == NQ - 1 else par), k * 4 + (s + 1)
                if q == 0 and i == 0:
                    pe.wait_ge(stacked, (k + 2) * (16 * 2 * PARTS))
                wait(pe, s_read, n * UNITS + (i - 1))
                for pair, j, at in unit_parts(i):
                    w = HALF * (j + 1)
                    for a in range(2):
                        last = mm(s_ps[HALF * a:HALF * (a + 1), (q + i) % 2, at:at + w],
                                  qs[sp_][0:ROWS, HQ // 2 * q + pair, j, a, :],
                                  ks[sp_][0:ROWS, HQ * q + 2 * pair + a, 0:w], start=True, stop=True)
                last.then_inc(s_full, 1)

            def outputs(k, s, lag, tiles, par):
                q, vp, n = (s - lag) % NQ, (1 - par if s < lag else par), k * 4 + (s - lag)
                u = {0: 1, 1: 3, 2: 4}[tiles[0]]
                pe.wait_ge(exp_ok, n * PAIRS + (u + 1))
                if tiles[0] == 0:
                    wait(pe, yT_ok, n)
                for j in tiles:
                    for hh in range(HQ):
                        u, bank, at = next((u, b_, a_) for u in range(PAIRS) for b_, a_, h_, j_ in pair_parts(u)
                                           if (h_, j_) == (hh, j))
                        last = mm(pv_ps[32 * hh:32 * (hh + 1), P * j:T], vv[vp][:, j, HQ * q + hh, :],
                                  probs[u][:, bank, at:at + T - P * j], start=j == 0, stop=j == 2,
                                  skip_group_check=True)
                last.then_inc(pv_ok, 1)

            def step(k, s, par):
                st, _, ss = has(k, s)
                for u in range(PAIRS):
                    if st:
                        transposed_scores(k, s, u, par)
                    if ss:
                        scores(k, s, 2 * u, par)
                    for name in step_fills(k, s, u):
                        if name[0] == "M":
                            fill(k, name, s)
                    if u == 0 and has_pv(k, s):
                        outputs(k, s, 2, [1, 3], par)
                    if u == 1 and has_pv(k, s):
                        outputs(k, s, 2, [2], par)
                    if u == 3 and st:
                        outputs(k, s, 1, [0], par)
                    if ss and 2 * u + 1 < UNITS:
                        scores(k, s, 2 * u + 1, par)
                    for name in step_fills(k, s, u):
                        if name[0] != "M":
                            fill(k, name, s)

            def tail():
                outputs(NB, 1, 2, [1, 3], 0)
                outputs(NB, 1, 2, [2], 0)
                for name in D_FILLS:
                    fill(NB, name, 0)

            programme(pe, prelude, step, tail)


def pair_parts(u):
    if u < 2:
        return [(b, 0, 2 * u + b, 0) for b in range(2)]
    if u < 4:
        return [(b, at, 2 * (u - 2) + b, j) for b in range(2) for at, j in ((0, 3), (P, 1))]
    return [(b, 2 * P * i, 2 * b + i, 2) for b in range(2) for i in range(2)]


def unit_parts(i):
    if i == 8:
        return [(0, 3, 0), (1, 3, 4 * HALF)]
    pair, i = divmod(i, 4)
    return [(pair, 7 - i, 0)] + ([(pair, i - 1, (8 - i) * HALF)] if i else [])


def kernel(L0_attn_x, L0_attn_W_dq, L0_attn_W_uq, L0_attn_W_dkv, L0_attn_W_uk, L0_attn_W_uv, L0_attn_W_o,
           L0_ffn_weight, L0_ffn_aux_weight1, L0_ffn_aux_weight2, L0_ffn_bias):
    import numpy as np
    import concourse.bacc as bacc
    from concourse.bass_utils import run_bass_kernel_spmd

    x, w_dq, w_uq, w_dkv, w_uk, w_uv, w_o, w1, a1, a2, bias = (np.asarray(a) for a in (
        L0_attn_x, L0_attn_W_dq, L0_attn_W_uq, L0_attn_W_dkv, L0_attn_W_uk, L0_attn_W_uv, L0_attn_W_o,
        L0_ffn_weight, L0_ffn_aux_weight1, L0_ffn_aux_weight2, L0_ffn_bias))
    lat, c = w_dq.shape

    def spread(w):
        return np.ascontiguousarray(w.reshape(lat, 8, 2, HS).transpose(0, 2, 3, 1).reshape(lat, c))

    arrays = {
        "x": x, "w_down": np.concatenate([w_dq, w_dkv]).T, "w_uq": w_uq, "w_uqT": spread(w_uq.T), "w_uk": w_uk,
        "w_dq": spread(w_dq), "w_uv": w_uv, "w_oT": w_o.T, "w_1T": w1.T, "w_a1": a1, "w_a2": a2, "bias": bias,
    }
    arrays = {name: np.ascontiguousarray(a) for name, a in arrays.items()}
    nc = bacc.Bacc("TRN2", target_bir_lowering=False, num_devices=1)
    args = [nc.dram_tensor(name, a.shape, mybir.dt.from_np(a.dtype), kind="ExternalInput").ap()
            for name, a in arrays.items()]
    out = nc.dram_tensor("out", x.shape, F32, kind="ExternalOutput").ap()
    block_kernel(nc, *args, out)
    r = run_bass_kernel_spmd(nc, [arrays], core_ids=[0])
    return r.results[0]["out"]
```
